# Optimizing a Trainium2 kernel written in Bass

```python
import numpy as np
import jax
import jax.numpy as jnp

def _softmax(x, axis=-1):
    return jax.nn.softmax(x, axis=axis)

def _gelu(x):
    return jax.nn.gelu(x, approximate=True)

def _silu(x):
    return jax.nn.silu(x)

def _sigmoid(x):
    return jax.nn.sigmoid(x)

def _layernorm(x, axis=-1, eps=1e-05):
    m = jnp.mean(x, axis=axis, keepdims=True)
    v = jnp.var(x, axis=axis, keepdims=True)
    return (x - m) / jnp.sqrt(v + eps)

def _scatter_add(tgt, idx, src, axis=0):
    return tgt.at[idx].add(src)

def _segment_sum(src, seg, n):
    return jax.ops.segment_sum(src, seg, n)
kernel_name = 'mk_adj_resnorm_d1_adj_r2_fcfa67'

def setup_inputs(seed: int=0):
    np.random.seed(seed)
    _w = jnp.asarray

    def _rec_inputs():
        import jax
        import jax.numpy as jnp
        _gk = jax.random.key(seed)
        x = -0.001003 + 1 * jax.random.normal(jax.random.fold_in(_gk, 1), (8192, 128), jnp.float32)
        _a = jax.random.bernoulli(jax.random.fold_in(_gk, 2), 0.000488281, (8192, 8192))
        _a = jnp.logical_or(_a, jnp.swapaxes(_a, -1, -2))
        _a = jnp.logical_or(_a, jnp.eye(8192, dtype=bool))
        _af = _a.astype(jnp.float32)
        _af = _af * jax.random.uniform(jax.random.fold_in(_gk, 3), (8192, 8192), jnp.float32, 0.05, 0.999999)
        adj = _af
        return (x, adj)
    x, adj = _rec_inputs()

    def _L0_gnn_setup():
        import jax, jax.numpy as jnp
        import numpy as np
        N = 3072
        HID = 128
        T = 350
        DENSITY = 0.05
        key = jax.random.key(seed)
        k1, k2, k3, k4, k5, k6 = jax.random.split(key, 6)
        h = jax.random.normal(k1, (N, HID), dtype=jnp.float32)
        a = jax.random.uniform(k2, (N, N), dtype=jnp.float32)
        mask = jax.random.uniform(k3, (N, N)) < DENSITY
        adj = jnp.where(mask, a, 0.0)
        simlar = jax.random.normal(k4, (N, N), dtype=jnp.float32)
        s = 1.0 / np.sqrt(HID)
        W_proj = jax.random.uniform(k5, (HID, HID), minval=-s, maxval=s, dtype=jnp.float32)
        b_proj = jnp.zeros((HID,), dtype=jnp.float32)
        W_gcn = jax.random.uniform(k6, (HID, HID), minval=-s, maxval=s, dtype=jnp.float32)
        b_gcn = jnp.zeros((HID,), dtype=jnp.float32)
        return {'h': h, 'adj': adj, 'simlar': simlar, 'W_proj': W_proj, 'b_proj': b_proj, 'W_gcn': W_gcn, 'b_gcn': b_gcn}
    _L0_gnn_all = _L0_gnn_setup()
    _L0_gnn_in = {k: v for k, v in _L0_gnn_all.items() if k in ('W_proj', 'b_proj', 'W_gcn', 'b_gcn')}
    del _L0_gnn_all
    return {'x': x, 'adj': adj, 'L0_gnn_W_proj': _L0_gnn_in['W_proj'], 'L0_gnn_b_proj': _L0_gnn_in['b_proj'], 'L0_gnn_W_gcn': _L0_gnn_in['W_gcn'], 'L0_gnn_b_gcn': _L0_gnn_in['b_gcn']}

def reference(x, adj, L0_gnn_W_proj, L0_gnn_b_proj, L0_gnn_W_gcn, L0_gnn_b_gcn):
    import jax
    import jax.numpy as jnp

    def _L0_gnn_ref(h, adj, simlar, W_proj, b_proj, W_gcn, b_gcn):
        import jax, jax.numpy as jnp
        import numpy as np
        N = 3072
        HID = 128
        T = 350
        DENSITY = 0.05
        sim = jnp.tanh(adj * simlar)
        filt = sim * (adj > 0).astype(sim.dtype)
        vals, idx = jax.lax.top_k(filt, T)
        nnz = jnp.sum(filt != 0, axis=1)
        keep = jnp.arange(T)[None, :] < nnz[:, None]
        rows = jnp.arange(filt.shape[0])[:, None]
        new_adj = jnp.zeros_like(filt).at[rows, idx].set(jnp.where(keep, vals, 0.0))
        h2 = jnp.tanh(h @ W_proj + b_proj)
        feat = jax.nn.relu(new_adj @ (h2 @ W_gcn) + b_gcn)
        return feat
    x = _layernorm(x + _L0_gnn_ref(x, adj, adj, L0_gnn_W_proj, L0_gnn_b_proj, L0_gnn_W_gcn, L0_gnn_b_gcn), axis=-1)
    return x

_drawn_inputs = setup_inputs


def setup_inputs(seed=0):
    import zlib

    import numpy as np

    out = dict(_drawn_inputs(seed))
    spreads = {'L0_gnn_b_proj': (0.0, 0.1), 'L0_gnn_b_gcn': (0.0, 0.1)}
    factors = {}
    for name, (base, spread) in spreads.items():
        noise = np.random.default_rng([zlib.crc32(name.encode()), seed]).standard_normal(out[name].shape)
        drawn = base * np.exp(spread * noise) if base else spread * noise
        out[name] = jnp.asarray(drawn.astype(out[name].dtype))
    for name, factor in factors.items():
        out[name] = (out[name] * factor).astype(out[name].dtype)
    return out
```

```python
import concourse.bass as bass
from concourse import mybir
from contextlib import ExitStack


def graph_layer_kernel(nc, x, adj, w_proj, b_proj, w_gcn, b_gcn, out):
    f32 = mybir.dt.float32
    i32 = mybir.dt.int32
    ALU = mybir.AluOpType
    ACT = mybir.ActivationFunctionType
    AX = mybir.AxisListType

    P = 128
    N, D = x.shape
    TOP = 350
    EPS = 1e-5
    CHUNK = 2048
    BLOCKS = CHUNK // P
    CHUNKS = N // CHUNK
    TILES = 4
    SUPERS = N // (TILES * P)
    GROUPS = SUPERS * CHUNKS
    Q = 4
    QW = CHUNK // Q
    VEC_TILES = [0, 2]
    PE_TILES = [t for t in range(TILES) if t not in VEC_TILES]
    NV, NP = len(VEC_TILES), len(PE_TILES)
    SLOTS = 2 * TILES
    SURE = TOP // Q
    ALL_TILES = N // P
    DUMMIES = -TOP % 8
    ROUNDS = (TOP + DUMMIES) // 8

    ctx = ExitStack()
    with ctx:
        def sb(name, shape, dt=f32):
            return ctx.enter_context(nc.sbuf_tensor(name, shape, dt))

        def pb(name, shape):
            return ctx.enter_context(nc.psum_tensor(name, shape, f32))

        def sem(name):
            return ctx.enter_context(nc.semaphore(name))

        slots = sb("slots", [P, SLOTS * CHUNK + 8])
        adjT = sb("adjT", [P, 2, BLOCKS, TILES, P])
        sqT = sb("sqT", [P, 2, CHUNK])
        g_sb = sb("g_sb", [P, CHUNKS, BLOCKS, D])
        xT = sb("xT", [P, 2, 4 * P])
        h2T = sb("h2T", [P, 2, 4 * P])
        ident = sb("ident", [P, P])
        wp_sb = sb("wp_sb", [P, D])
        wg_sb = sb("wg_sb", [P, D])
        bp_sb = sb("bp_sb", [P, 1])
        bg_sb = sb("bg_sb", [P, 1])
        counts = sb("counts", [P, GROUPS * TILES])
        count_sums = sb("count_sums", [P, SUPERS, TILES])
        count_max = sb("count_max", [P, 1])
        count_top = sb("count_top", [P, 1])
        over = sb("over", [P, 1], i32)
        half_sum = sb("half_sum", [P, TILES * P])
        featT = sb("featT", [P, TILES * P])
        x_tile = sb("x_tile", [P, TILES, D])
        y_tile = sb("y_tile", [P, TILES, D])
        out_tile = sb("out_tile", [P, TILES, D])
        stats = sb("stats", [P, TILES, 6])
        mean_var = sb("mean_var", [P, TILES, 2])
        var_eps = sb("var_eps", [P, TILES])
        rstd = sb("rstd", [P, TILES])
        minus_half = sb("minus_half", [P, TILES])
        eps_tile = sb("eps_tile", [P, TILES])
        wait_pad = sb("wait_pad", [P, 1])
        x_in = adjT[:, 1].rearrange("p c t i -> p (c t i)").rearrange("p (k d) -> p k d", d=D)

        top8 = sb("top8", [P, 8])
        gen_sq = slots[:, 0:N]
        gen_rest = slots[:, N:N + DUMMIES + N]
        gen_filt = adjT[:, 0].rearrange("p c t i -> p (c t i)")
        gen_adjT = adjT[:, 1].rearrange("p c t i -> p (c t i)")

        ps_turn = pb("ps_turn", [P, BLOCKS * P])
        ps_acc = pb("ps_acc", [P, 2, TILES * P])
        ps_epi = pb("ps_epi", [P, TILES * P])

        ident_zero = sem("ident_zero")
        ident_ready = sem("ident_ready")
        half_const = sem("half_const")
        weights_loaded = sem("weights_loaded")
        x_in_loaded = [sem(f"x_in_loaded{c}") for c in range(CHUNKS)]
        x_turned = sem("x_turned")
        xT_ready = sem("xT_ready")
        proj_done = sem("proj_done")
        h2T_ready = sem("h2T_ready")
        gcn_done = sem("gcn_done")
        g_ready = sem("g_ready")
        unit_loaded = [sem(f"unit_loaded{s}") for s in range(SLOTS)]
        squared = sem("squared")
        counted = sem("counted")
        pe_turned = sem("pe_turned")
        vec_turned = sem("vec_turned")
        tanh_of_pe = sem("tanh_of_pe")
        tanh_of_vec = sem("tanh_of_vec")
        group_used = sem("group_used")
        acc_read = sem("acc_read")
        feat_turned = sem("feat_turned")
        x_tile_loaded = sem("x_tile_loaded")
        y_ready = sem("y_ready")
        stats_ready = sem("stats_ready")
        mean_ready = sem("mean_ready")
        eps_added = sem("eps_added")
        rstd_ready = sem("rstd_ready")
        normed = sem("normed")
        stored = sem("stored")
        sums_ready = sem("sums_ready")
        max_ready = sem("max_ready")
        top_ready = sem("top_ready")
        over_ready = sem("over_ready")
        gen_loaded = sem("gen_loaded")
        gen_dummies = sem("gen_dummies")
        gen_squared = sem("gen_squared")
        gen_tanh = sem("gen_tanh")
        gen_top8 = sem("gen_top8")
        gen_taken = sem("gen_taken")
        gen_kept = sem("gen_kept")
        gen_turned = sem("gen_turned")
        gen_copied = sem("gen_copied")
        gen_products = sem("gen_products")
        gen_feat = sem("gen_feat")
        gen_feat_turned = sem("gen_feat_turned")
        gen_y = sem("gen_y")
        gen_stats = sem("gen_stats")
        gen_mean = sem("gen_mean")
        gen_eps = sem("gen_eps")
        gen_rstd = sem("gen_rstd")
        gen_normed = sem("gen_normed")
        gen_stored = sem("gen_stored")

        block = ctx.enter_context(nc.Block())

        def group(st, gc):
            return st * CHUNKS + gc

        def slot_of(gc, t):
            s = (gc % 2) * TILES + t
            return slots[:, s * CHUNK:(s + 1) * CHUNK]

        @block.sync
        def _(sp):
            def load_x():
                xv = x.rearrange("(k p c) d -> k p (c d)", p=P, c=BLOCKS)
                for k in range(CHUNKS):
                    sp.dma_start(x_in[:, k * BLOCKS:(k + 1) * BLOCKS, :].rearrange("p c d -> p (c d)"),
                                 xv[k]).then_inc(x_in_loaded[k], 16)

            def load_unit(st, gc, t, first):
                s = (gc % 2) * TILES + t
                rows = bass.ds(st * (TILES * P) + t * P, P)
                if not first:
                    sp.wait_ge(counted, (group(st, gc) - 2) * TILES + t + 1)
                if t in VEC_TILES:
                    for q in range(Q):
                        cols = slice(gc * CHUNK + q * QW, gc * CHUNK + (q + 1) * QW)
                        sp.dma_start(slot_of(gc, t)[32 * q:32 * q + 32, :].rearrange("a (r f) -> a r f", r=Q),
                                     adj[rows, cols].rearrange("(r a) f -> a r f", r=Q)
                                     ).then_inc(unit_loaded[s], 16)
                else:
                    sp.dma_start(slot_of(gc, t), adj[rows, gc * CHUNK:(gc + 1) * CHUNK]
                                 ).then_inc(unit_loaded[s], 16)

            def load_x_tile(st):
                rows = bass.ds((st - 1) * (TILES * P), TILES * P)
                sp.wait_ge(y_ready, st)
                sp.dma_start(x_tile[:], x[rows, :].rearrange("(t p) d -> p t d", p=P)).then_inc(x_tile_loaded, 16)

            load_x()
            for gc in range(CHUNKS):
                for t in range(TILES):
                    load_unit(0, gc, t, first=gc < 2)
            with sp.Fori(1, SUPERS) as st:
                load_x_tile(st)
                for gc in range(CHUNKS):
                    for t in range(TILES):
                        load_unit(st, gc, t, first=False)
            load_x_tile(SUPERS)

            sp.wait_ge(over_ready, 1)
            general = sp.value_load(over[0:1, 0:1], min_val=0, max_val=1)
            with sp.If(general > 0):
                sp.wait_ge(stored, (SUPERS + 1) * 16)
                with sp.Fori(0, ALL_TILES) as tile:
                    sp.wait_ge(gen_stored, tile * 16 + 16)
                    sp.dma_start(gen_sq, adj[bass.ds(tile * P, P), :]).then_inc(gen_loaded, 16)
                    sp.dma_start(x_tile[:, 0, :], x[bass.ds(tile * P, P), :]).then_inc(gen_loaded, 16)
                    sp.wait_ge(gen_normed, tile + 1)
                    sp.dma_start(out[bass.ds(tile * P, P), :], out_tile[:, 0, :]).then_inc(gen_stored, 16)
                sp.wait_ge(gen_stored, (ALL_TILES + 1) * 16)

        @block.gpsimd
        def _(pool):
            pool.memset(ident[:], 0.0).then_inc(ident_zero, 1)
            pool.memset(minus_half[:], -0.5).then_inc(half_const, 1)
            pool.memset(eps_tile[:], EPS).then_inc(half_const, 1)
            pool.wait_ge(ident_zero, 1)
            pool.affine_select(out=ident[:], in_=ident[:], compare_op=ALU.not_equal, fill=1.0, base=0,
                               pattern=[[-1, P]], channel_multiplier=1).then_inc(ident_ready, 1)
            pool.dma_start(wp_sb[:], w_proj).then_inc(weights_loaded, 16)
            pool.dma_start(wg_sb[:], w_gcn).then_inc(weights_loaded, 16)
            pool.dma_start(bp_sb[:], b_proj.rearrange("(p o) -> p o", o=1)).then_inc(weights_loaded, 16)
            pool.dma_start(bg_sb[:], b_gcn.rearrange("(p o) -> p o", o=1)).then_inc(weights_loaded, 16)
            pool.wait_ge(half_const, 2)
            pool.sem_inc(y_ready, 1)
            pool.sem_inc(feat_turned, 1)
            pool.sem_inc(stored, 16)
            pool.sem_inc(gen_copied, 1)
            pool.sem_inc(gen_stored, 16)

            def invert_std(st):
                pool.wait_ge(mean_ready, st * TILES + TILES)
                pool.tensor_tensor(var_eps[:], mean_var[:, :, 1], eps_tile[:], ALU.add).then_inc(eps_added, 1)
                pool.wait_ge(eps_added, st + 1)
                pool.tensor_tensor(rstd[:], var_eps[:], minus_half[:], ALU.pow).then_inc(rstd_ready, 1)

            with pool.Fori(0, SUPERS) as st:
                invert_std(st)
            pool.wait_ge(max_ready, 1)
            pool.partition_all_reduce(count_top[:], count_max[:], P, bass.bass_isa.ReduceOp.max).then_inc(top_ready, 1)

            pool.wait_ge(over_ready, 1)
            general = pool.value_load(over[0:1, 0:1], min_val=0, max_val=1)
            with pool.If(general > 0):
                with pool.Fori(0, ALL_TILES) as tile:
                    pool.wait_ge(gen_mean, tile + 1)
                    pool.tensor_tensor(var_eps[:, 0:1], mean_var[:, 0, 1:2], eps_tile[:, 0:1], ALU.add
                                       ).then_inc(gen_eps, 1)
                    pool.wait_ge(gen_eps, tile + 1)
                    pool.tensor_tensor(rstd[:, 0:1], var_eps[:, 0:1], minus_half[:, 0:1], ALU.pow
                                       ).then_inc(gen_rstd, 1)

        @block.scalar
        def _(act):
            act.wait_ge(weights_loaded, 64)
            for n in range(CHUNKS * 4):
                act.wait_ge(proj_done, n + 1)
                if n >= 2:
                    act.wait_ge(gcn_done, n - 1)
                act.activation(h2T[:, n % 2, :], ps_acc[:, n % 2, :], ACT.Tanh, bias=bp_sb[:, 0:1]
                               ).then_inc(h2T_ready, 1)

            def tanh_group(st, gc, no_user):
                if not no_user:
                    act.wait_ge(group_used, group(st, gc) - 1)
                if no_user and gc == 1:
                    act.wait_ge(x_turned, CHUNKS * 4)
                for t in range(TILES):
                    if t in VEC_TILES:
                        n = VEC_TILES.index(t)
                        act.wait_ge(vec_turned, group(st, gc) * NV + n + 1)
                        src = sqT[:, (gc * NV + n) % 2, :].rearrange("p (r c a) -> p c r a", r=Q, c=BLOCKS)
                        act.activation(adjT[:, gc % 2, :, t, :].rearrange("p c (r a) -> p c r a", r=Q), src,
                                       ACT.Tanh).then_inc(tanh_of_vec, 1)
                    else:
                        n = PE_TILES.index(t)
                        act.wait_ge(pe_turned, group(st, gc) * NP + n + 1)
                        act.activation(adjT[:, gc % 2, :, t, :],
                                       ps_turn[:].rearrange("p (c i) -> p c i", c=BLOCKS),
                                       ACT.Tanh).then_inc(tanh_of_pe, 1)
                    act.activation(slot_of(gc, t), slot_of(gc, t), ACT.Sign,
                                   accum_out=counts[:, bass.ds(group(st, gc) * TILES + t, 1)]
                                   ).then_inc(counted, 1)

            for gc in range(CHUNKS):
                tanh_group(0, gc, no_user=gc < 2)
            def store(st):
                act.wait_ge(normed, st)
                rows = bass.ds((st - 1) * (TILES * P), TILES * P)
                act.dma_start(out[rows, :].rearrange("(t p) d -> p t d", p=P), out_tile[:]).then_inc(stored, 16)

            with act.Fori(1, SUPERS) as st:
                for gc in range(CHUNKS):
                    tanh_group(st, gc, no_user=False)
                store(st)
            store(SUPERS)
            act.wait_ge(stored, (SUPERS + 1) * 16)

            act.wait_ge(over_ready, 1)
            general = act.value_load(over[0:1, 0:1], min_val=0, max_val=1)
            with act.If(general > 0):
                with act.Fori(0, ALL_TILES) as tile:
                    act.wait_ge(gen_squared, tile + 1)
                    act.activation(gen_filt, gen_sq, ACT.Tanh).then_inc(gen_tanh, 1)
                    act.activation(gen_rest[:, DUMMIES:], gen_sq, ACT.Tanh).then_inc(gen_tanh, 1)
                    for k in range(CHUNKS):
                        act.wait_ge(gen_turned, tile * CHUNKS + k + 1)
                        act.activation(gen_adjT[:, k * CHUNK:(k + 1) * CHUNK], ps_turn[:], ACT.Copy
                                       ).then_inc(gen_copied, 1)

        @block.tensor
        def _(pe):
            def turn_x(n):
                k, c0 = n // 4, 4 * (n % 4)
                pe.wait_ge(x_in_loaded[k], 16)
                if n >= 2:
                    pe.wait_ge(xT_ready, n - 1)
                for c in range(4):
                    mm = pe.transpose(ps_turn[:, (n % 2) * 512 + c * P:(n % 2) * 512 + (c + 1) * P],
                                      x_in[:, k * BLOCKS + c0 + c, :], ident[:])
                mm.then_inc(x_turned, 1)

            def project(n):
                pe.wait_ge(xT_ready, n + 1)
                if n >= 2:
                    pe.wait_ge(h2T_ready, n - 1)
                pe.matmul(ps_acc[:, n % 2, :], wp_sb[:], xT[:, n % 2, :], start=True, stop=True
                          ).then_inc(proj_done, 1)

            def gcn(n):
                pe.wait_ge(h2T_ready, n + 1)
                if n >= 2:
                    pe.wait_ge(g_ready, n - 1)
                for c in range(4):
                    lo = 1024 + (n % 2) * 512 + c * P
                    mm = pe.matmul(ps_turn[:, lo:lo + P], h2T[:, n % 2, c * P:(c + 1) * P], wg_sb[:],
                                   start=True, stop=True)
                mm.then_inc(gcn_done, 1)

            pe.wait_ge(ident_ready, 1)
            pe.wait_ge(weights_loaded, 64)
            for n in range(CHUNKS * 4 + 2):
                if n < CHUNKS * 4:
                    turn_x(n)
                if 1 <= n <= CHUNKS * 4:
                    project(n - 1)
                if n >= 2:
                    gcn(n - 2)

            def turn_unit(st, gc, t, first):
                n = PE_TILES.index(t)
                pe.wait_ge(squared, group(st, gc) * TILES + t + 1)
                if not (first and n == 0):
                    pe.wait_ge(tanh_of_pe, group(st, gc) * NP + n)
                cols = slot_of(gc, t).rearrange("p (j c) -> p c j", c=BLOCKS)
                for c in range(BLOCKS):
                    mm = pe.transpose(ps_turn[:, c * P:(c + 1) * P], cols[:, c, :], ident[:])
                mm.then_inc(pe_turned, 1)

            def multiply(st, gc, c0, c1):
                k = (gc - 1) % CHUNKS
                for c in range(c0, c1):
                    mm = pe.matmul(ps_acc[:, k // 2, :], g_sb[:, k, c, :],
                                   adjT[:, (gc - 1) % 2, c].rearrange("p t i -> p (t i)"),
                                   start=(k % 2 == 0 and c == 0), stop=(k % 2 == 1 and c == BLOCKS - 1))
                if c1 == BLOCKS:
                    mm.then_inc(group_used, 1)

            def begin_group(st, gc, first):
                k = (gc - 1) % CHUNKS
                pe.wait_ge(tanh_of_pe, group(st, gc) * NP)
                pe.wait_ge(tanh_of_vec, group(st, gc) * NV)
                if not first:
                    if k == 0:
                        pe.wait_ge(acc_read, st * 2 - 1)
                    if k == 2:
                        pe.wait_ge(acc_read, st * 2)

            def turn_feat(st):
                pe.wait_ge(acc_read, st * 2)
                pe.wait_ge(y_ready, st)
                for t in range(TILES):
                    mm = pe.transpose(ps_epi[:, t * P:(t + 1) * P], featT[:, t * P:(t + 1) * P], ident[:])
                mm.then_inc(feat_turned, 1)

            STEP = BLOCKS // NP if NP else BLOCKS

            def super_tile(st, first):
                for gc in range(CHUNKS):
                    has_group = not (first and gc == 0)
                    if has_group:
                        begin_group(st, gc, first)
                    for n in range(max(NP, 1)):
                        if has_group:
                            multiply(st, gc, n * STEP, (n + 1) * STEP)
                        if n < NP:
                            turn_unit(st, gc, PE_TILES[n], first=first and gc == 0)
                    if gc == 2 and not first:
                        turn_feat(st)

            pe.wait_ge(g_ready, CHUNKS * 4)
            super_tile(0, True)
            with pe.Fori(1, SUPERS) as st:
                super_tile(st, False)
            begin_group(SUPERS, 0, False)
            multiply(SUPERS, 0, 0, BLOCKS)
            turn_feat(SUPERS)

            pe.wait_ge(over_ready, 1)
            general = pe.value_load(over[0:1, 0:1], min_val=0, max_val=1)
            with pe.If(general > 0):
                with pe.Fori(0, ALL_TILES) as tile:
                    pe.wait_ge(gen_kept, tile + 1)
                    for k in range(CHUNKS):
                        pe.wait_ge(gen_copied, tile * CHUNKS + k + 1)
                        cols = gen_filt[:, k * CHUNK:(k + 1) * CHUNK].rearrange("p (j c) -> p c j", c=BLOCKS)
                        for c in range(BLOCKS):
                            mm = pe.transpose(ps_turn[:, c * P:(c + 1) * P], cols[:, c, :], ident[:])
                        mm.then_inc(gen_turned, 1)
                    pe.wait_ge(gen_copied, tile * CHUNKS + CHUNKS + 1)
                    for k in range(CHUNKS):
                        for c in range(BLOCKS):
                            lo = (k * BLOCKS + c) * P
                            mm = pe.matmul(ps_acc[:, 0, 0:P], g_sb[:, k, c, :], gen_adjT[:, lo:lo + P],
                                           start=(k == 0 and c == 0),
                                           stop=(k == CHUNKS - 1 and c == BLOCKS - 1))
                    mm.then_inc(gen_products, 1)
                    pe.wait_ge(gen_feat, tile + 1)
                    pe.transpose(ps_epi[:, 0:P], featT[:, 0:P], ident[:]).then_inc(gen_feat_turned, 1)

        @block.vector
        def _(dve):
            for n in range(CHUNKS * 4 + 2):
                if n < CHUNKS * 4:
                    dve.wait_ge(x_turned, n + 1)
                    if n >= 2:
                        dve.wait_ge(proj_done, n - 1)
                    dve.tensor_copy(xT[:, n % 2, :], ps_turn[:, (n % 2) * 512:(n % 2) * 512 + 512]
                                    ).then_inc(xT_ready, 1)
                if n >= 2:
                    m = n - 2
                    dve.wait_ge(gcn_done, m + 1)
                    lo = 1024 + (m % 2) * 512
                    dve.tensor_copy(g_sb[:, m // 4, 4 * (m % 4):4 * (m % 4) + 4, :],
                                    ps_turn[:, lo:lo + 512].rearrange("p (c d) -> p c d", d=D)
                                    ).then_inc(g_ready, 1)

            def square(st, gc, t):
                s = (gc % 2) * TILES + t
                per_load = 16 * (Q if t in VEC_TILES else 1)
                dve.wait_ge(unit_loaded[s], (st * (CHUNKS // 2) + gc // 2 + 1) * per_load)
                dve.scalar_tensor_tensor(out=slot_of(gc, t), in0=slot_of(gc, t), scalar=0.0, in1=slot_of(gc, t),
                                         op0=ALU.max, op1=ALU.mult).then_inc(squared, 1)

            def turn(st, gc, t, first):
                n = VEC_TILES.index(t)
                dve.wait_ge(squared, group(st, gc) * TILES + t + 1)
                if not (first and n < 2):
                    dve.wait_ge(tanh_of_vec, group(st, gc) * NV + n - 1)
                dve.transpose(sqT[:, (gc * NV + n) % 2, :].rearrange("p (r c a) -> p r c a", r=Q, c=BLOCKS),
                              slot_of(gc, t).rearrange("p (r b c) -> p r c b", r=Q, c=BLOCKS)
                              ).then_inc(vec_turned, 1)

            def read_first_half(st):
                dve.wait_ge(group_used, st * CHUNKS + 2)
                dve.tensor_scalar(half_sum[:], ps_acc[:, 0, :], bg_sb[:, 0:1], None, ALU.add).then_inc(acc_read, 1)

            def read_second_half(st):
                dve.wait_ge(group_used, st * CHUNKS)
                dve.wait_ge(acc_read, st * 2 - 1)
                dve.wait_ge(feat_turned, st)
                dve.tensor_tensor(featT[:], ps_acc[:, 1, :], half_sum[:], ALU.add).then_inc(acc_read, 1)

            def add_x(st):
                dve.wait_ge(feat_turned, st + 1)
                dve.wait_ge(x_tile_loaded, st * 16)
                yt = y_tile[:].rearrange("p t d -> p (t d)")
                dve.scalar_tensor_tensor(out=yt, in0=ps_epi[:], scalar=0.0,
                                         in1=x_tile[:].rearrange("p t d -> p (t d)"),
                                         op0=ALU.max, op1=ALU.add).then_inc(y_ready, 1)
                dve.wait_ge(y_ready, st + 1)
                for t in range(TILES):
                    dve.bn_stats(stats[:, t, :], y_tile[:, t, :]).then_inc(stats_ready, 1)
                dve.wait_ge(stats_ready, st * TILES)
                dve.memset(wait_pad[:], 0.0)
                for t in range(TILES):
                    dve.bn_aggr(mean_var[:, t, :], stats[:, t, :]).then_inc(mean_ready, 1)

            def norm(st):
                dve.wait_ge(rstd_ready, st)
                dve.wait_ge(mean_ready, st * TILES)
                dve.wait_ge(stored, st * 16)
                for t in range(TILES):
                    ins = dve.tensor_scalar(out_tile[:, t, :], y_tile[:, t, :], mean_var[:, t, 0:1], rstd[:, t:t + 1],
                                            ALU.subtract, ALU.mult)
                ins.then_inc(normed, 1)

            def super_tile(st, first):
                for gc in range(CHUNKS):
                    late = None
                    for t in range(TILES):
                        square(st, gc, t)
                        if late is not None:
                            turn(st, gc, late, first and gc == 0)
                        late = t if t in VEC_TILES else None
                    if late is not None:
                        turn(st, gc, late, first and gc == 0)
                    if gc == 1 and not first:
                        read_second_half(st)
                    if gc == 2 and not first:
                        add_x(st)
                    if gc == 3:
                        if not first:
                            norm(st)
                        read_first_half(st)

            dve.wait_ge(weights_loaded, 64)
            super_tile(0, True)
            with dve.Fori(1, SUPERS) as st:
                super_tile(st, False)
            read_second_half(SUPERS)
            add_x(SUPERS)
            norm(SUPERS)
            dve.wait_ge(counted, GROUPS * TILES)
            dve.tensor_reduce(count_sums[:], counts[:].rearrange("p (s k t) -> p s t k", k=CHUNKS, t=TILES),
                              AX.X, ALU.add).then_inc(sums_ready, 1)
            dve.wait_ge(sums_ready, 1)
            dve.tensor_reduce(count_max[:], count_sums[:].rearrange("p s t -> p (s t)"), AX.X, ALU.max
                              ).then_inc(max_ready, 1)
            dve.wait_ge(top_ready, 1)
            dve.tensor_scalar(over[:], count_top[:], SURE + 0.5, None, ALU.is_gt).then_inc(over_ready, 1)

            dve.wait_ge(over_ready, 1)
            general = dve.value_load(over[0:1, 0:1], min_val=0, max_val=1)
            with dve.If(general > 0):
                with dve.Fori(0, ALL_TILES) as tile:
                    dve.wait_ge(gen_loaded, tile * 32 + 32)
                    if DUMMIES:
                        dve.memset(gen_rest[:, 0:DUMMIES], 2.0)
                    dve.scalar_tensor_tensor(out=gen_sq, in0=gen_sq, scalar=0.0, in1=gen_sq,
                                             op0=ALU.max, op1=ALU.mult).then_inc(gen_squared, 1)
                    dve.wait_ge(gen_tanh, tile * 2 + 2)
                    dve.memset(wait_pad[:], 0.0)
                    with dve.Fori(0, ROUNDS) as rnd:
                        dve.max(top8[:], gen_rest).then_inc(gen_top8, 1)
                        dve.wait_ge(gen_top8, tile * ROUNDS + rnd + 1)
                        dve.memset(wait_pad[:], 0.0)
                        dve.match_replace(gen_rest, top8[:], gen_rest, 0.0).then_inc(gen_taken, 1)
                        dve.wait_ge(gen_taken, tile * ROUNDS + rnd + 1)
                        dve.memset(wait_pad[:], 0.0)
                    dve.tensor_tensor(gen_filt, gen_filt, gen_rest[:, DUMMIES:], ALU.subtract
                                      ).then_inc(gen_kept, 1)
                    dve.wait_ge(gen_products, tile + 1)
                    dve.tensor_scalar(featT[:, 0:P], ps_acc[:, 0, 0:P], bg_sb[:, 0:1], None, ALU.add
                                      ).then_inc(gen_feat, 1)
                    dve.wait_ge(gen_feat_turned, tile + 1)
                    dve.scalar_tensor_tensor(out=y_tile[:, 0, :], in0=ps_epi[:, 0:P], scalar=0.0,
                                             in1=x_tile[:, 0, :], op0=ALU.max, op1=ALU.add).then_inc(gen_y, 1)
                    dve.wait_ge(gen_y, tile + 1)
                    dve.bn_stats(stats[:, 0, :], y_tile[:, 0, :]).then_inc(gen_stats, 1)
                    dve.wait_ge(gen_stats, tile + 1)
                    dve.memset(wait_pad[:], 0.0)
                    dve.bn_aggr(mean_var[:, 0, :], stats[:, 0, :]).then_inc(gen_mean, 1)
                    dve.wait_ge(gen_rstd, tile + 1)
                    dve.wait_ge(gen_mean, tile + 1)
                    dve.tensor_scalar(out_tile[:, 0, :], y_tile[:, 0, :], mean_var[:, 0, 0:1], rstd[:, 0:1],
                                      ALU.subtract, ALU.mult).then_inc(gen_normed, 1)


_INS = ['x', 'adj', 'L0_gnn_W_proj', 'L0_gnn_b_proj', 'L0_gnn_W_gcn', 'L0_gnn_b_gcn']
_OUTS = [((8192, 128), 'float32')]


def kernel(**inputs):
    import numpy as _np
    import concourse.bacc as _bacc
    from concourse import mybir as _mybir
    from concourse.bass_utils import run_bass_kernel_spmd as _run

    nc = _bacc.Bacc("TRN2", target_bir_lowering=False, num_devices=1)
    arrays, args = {}, []
    for name in _INS:
        a = _np.ascontiguousarray(inputs[name])
        arrays[f"in_{name}_dram"] = a
        args.append(nc.dram_tensor(f"in_{name}_dram", a.shape, _mybir.dt.from_np(a.dtype), kind="ExternalInput").ap())
    for i, (shape, dtype) in enumerate(_OUTS):
        dt = _mybir.dt.from_np(_np.dtype(dtype))
        args.append(nc.dram_tensor(f"out_{i}_dram", shape, dt, kind="ExternalOutput").ap())
    graph_layer_kernel(nc, *args)
    r = _run(nc, [arrays], core_ids=[0])
    got = tuple(r.results[0][f"out_{i}_dram"] for i in range(len(_OUTS)))
    return got[0]
```

```python
from contextlib import ExitStack

import concourse.bass as bass
from concourse import mybir


def graph_layer_kernel(nc, x, adj, w_proj, b_proj, w_gcn, b_gcn, out):
    f32 = mybir.dt.float32
    i32 = mybir.dt.int32
    ALU = mybir.AluOpType
    ACT = mybir.ActivationFunctionType
    AX = mybir.AxisListType

    P = 128
    N, D = x.shape
    TOP = 350
    EPS = 1e-5
    CHUNK = 2048
    BLOCKS = CHUNK // P
    CHUNKS = N // CHUNK
    TILES = 4
    SUPERS = N // (TILES * P)
    GROUPS = SUPERS * CHUNKS
    Q = 4
    QW = CHUNK // Q
    VEC = [[1, 2, 3], [1, 2, 3], [1, 2, 3], [1, 2, 3]]
    PET = [[t for t in range(TILES) if t not in v] for v in VEC]
    NV, NP = sum(map(len, VEC)), sum(map(len, PET))
    TURN_AT = [0]
    SLOTS = 2 * TILES
    SQ_BUFS = 4
    PIECES = CHUNKS * 4
    VEC_EARLY = [3, 5, 7, 9, 11, 13, 15]
    TANH_EARLY = [11, 13]
    SURE = TOP // Q
    ALL_TILES = N // P
    DUMMIES = -TOP % 8
    ROUNDS = (TOP + DUMMIES) // 8

    ctx = ExitStack()
    with ctx:
        def sb(name, shape, dt=f32):
            return ctx.enter_context(nc.sbuf_tensor(name, shape, dt))

        def pb(name, shape):
            return ctx.enter_context(nc.psum_tensor(name, shape, f32))

        def sem(name):
            return ctx.enter_context(nc.semaphore(name))

        slots = sb("slots", [P, SLOTS * CHUNK + 8])
        adjT = sb("adjT", [P, 2, BLOCKS, TILES, P])
        sqT = sb("sqT", [P, SQ_BUFS, CHUNK])
        g_sb = sb("g_sb", [P, CHUNKS, BLOCKS, D])
        ident = sb("ident", [P, P])
        wp_sb = sb("wp_sb", [P, D])
        wg_sb = sb("wg_sb", [P, D])
        bp_sb = sb("bp_sb", [P, 1])
        bg_sb = sb("bg_sb", [P, 1])
        counts = sb("counts", [P, GROUPS * 2])
        count_sums = sb("count_sums", [P, SUPERS, 2])
        count_max = sb("count_max", [P, 1])
        count_top = sb("count_top", [P, 1])
        over = sb("over", [P, 1], i32)
        feat = sb("feat", [P, TILES * P])
        featT = sb("featT", [P, TILES * P])
        x_tile = sb("x_tile", [P, TILES, D])
        y_tile = sb("y_tile", [P, TILES, D])
        out_tile = sb("out_tile", [P, TILES, D])
        stats = sb("stats", [P, TILES, 6])
        mean_var = sb("mean_var", [P, TILES, 2])
        var_eps = sb("var_eps", [P, TILES])
        rstd = sb("rstd", [P, TILES])
        minus_one = sb("minus_one", [P, TILES])
        shift = sb("shift", [P, TILES])
        minus_mean = sb("minus_mean", [P, TILES])
        minus_half = sb("minus_half", [P, TILES])
        eps_tile = sb("eps_tile", [P, TILES])
        wait_pad = sb("wait_pad", [P, 1])
        xT = sqT[:, SQ_BUFS - 1, 0:1024].rearrange("p (b i) -> p b i", b=2)
        h2T = sqT[:, SQ_BUFS - 1, 1024:2048].rearrange("p (b i) -> p b i", b=2)
        x_in = adjT[:, 1].rearrange("p c t i -> p (c t i)").rearrange("p (k d) -> p k d", d=D)

        top8 = sb("top8", [P, 8])
        gen_sq = slots[:, 0:N]
        gen_rest = slots[:, N:N + DUMMIES + N]
        gen_filt = adjT[:, 0].rearrange("p c t i -> p (c t i)")
        gen_adjT = adjT[:, 1].rearrange("p c t i -> p (c t i)")

        ps_turn = pb("ps_turn", [P, BLOCKS * P])
        ps_acc = pb("ps_acc", [P, TILES * P])
        ps_proj = pb("ps_proj", [P, TILES * P])
        ps_epi = pb("ps_epi", [P, TILES * P])

        ident_zero = sem("ident_zero")
        ident_ready = sem("ident_ready")
        half_const = sem("half_const")
        w_proj_loaded = sem("w_proj_loaded")
        w_gcn_loaded = sem("w_gcn_loaded")
        biases_loaded = sem("biases_loaded")
        x_in_loaded = [sem(f"x_in_loaded{c}") for c in range(CHUNKS)]
        x_turned = sem("x_turned")
        xT_ready = sem("xT_ready")
        proj_done = sem("proj_done")
        h2T_ready = sem("h2T_ready")
        gcn_done = sem("gcn_done")
        g_ready = sem("g_ready")
        unit_loaded = [sem(f"unit_loaded{s}") for s in range(SLOTS)]
        squared = sem("squared")
        counted = sem("counted")
        pe_turned = sem("pe_turned")
        vec_turned = sem("vec_turned")
        tanh_of_pe = sem("tanh_of_pe")
        tanh_of_vec = sem("tanh_of_vec")
        group_used = sem("group_used")
        acc_read = sem("acc_read")
        feat_ready = sem("feat_ready")
        feat_turned = sem("feat_turned")
        x_tile_loaded = sem("x_tile_loaded")
        y_ready = sem("y_ready")
        stats_ready = sem("stats_ready")
        mean_ready = sem("mean_ready")
        eps_added = sem("eps_added")
        rstd_ready = sem("rstd_ready")
        minus_mean_ready = sem("minus_mean_ready")
        shift_ready = sem("shift_ready")
        normed = sem("normed")
        stored = sem("stored")
        sums_ready = sem("sums_ready")
        max_ready = sem("max_ready")
        top_ready = sem("top_ready")
        over_ready = sem("over_ready")
        gen_loaded = sem("gen_loaded")
        gen_dummies = sem("gen_dummies")
        gen_squared = sem("gen_squared")
        gen_tanh = sem("gen_tanh")
        gen_top8 = sem("gen_top8")
        gen_taken = sem("gen_taken")
        gen_kept = sem("gen_kept")
        gen_turned = sem("gen_turned")
        gen_copied = sem("gen_copied")
        gen_products = sem("gen_products")
        gen_feat = sem("gen_feat")
        gen_feat_turned = sem("gen_feat_turned")
        gen_y = sem("gen_y")
        gen_stats = sem("gen_stats")
        gen_mean = sem("gen_mean")
        gen_eps = sem("gen_eps")
        gen_rstd = sem("gen_rstd")
        gen_normed = sem("gen_normed")
        gen_stored = sem("gen_stored")

        block = ctx.enter_context(nc.Block())

        def group(st, gc):
            return st * CHUNKS + gc

        def vec_unit(st, gc, n):
            return st * NV + sum(map(len, VEC[:gc])) + n

        def pe_unit(st, gc, n):
            return st * NP + sum(map(len, PET[:gc])) + n

        SQUARE_ORDER = [PET[gc] + VEC[gc] for gc in range(CHUNKS)]

        def slot_of(gc, t):
            s = (gc % 2) * TILES + t
            return slots[:, s * CHUNK:(s + 1) * CHUNK]

        @block.sync
        def _(sp):
            def load_x(k):
                sp.dma_start(x_in[:, k * BLOCKS:(k + 1) * BLOCKS, :].rearrange("p c d -> p (c d)"),
                             x.rearrange("(k p c) d -> k p (c d)", p=P, c=BLOCKS)[k]).then_inc(x_in_loaded[k], 16)

            def load_unit(st, gc, t, first):
                s = (gc % 2) * TILES + t
                rows = bass.ds(st * (TILES * P) + t * P, P)
                if not first:
                    sp.wait_ge(counted, (group(st, gc) - 2) * 2 + t // 2 + 1)
                if t in VEC[gc]:
                    for q in range(Q):
                        cols = slice(gc * CHUNK + q * QW, gc * CHUNK + (q + 1) * QW)
                        sp.dma_start(slot_of(gc, t)[32 * q:32 * q + 32, :].rearrange("a (r f) -> a r f", r=Q),
                                     adj[rows, cols].rearrange("(r a) f -> a r f", r=Q)
                                     ).then_inc(unit_loaded[s], 16)
                else:
                    sp.dma_start(slot_of(gc, t), adj[rows, gc * CHUNK:(gc + 1) * CHUNK]
                                 ).then_inc(unit_loaded[s], 16)

            def load_x_tile(st):
                rows = bass.ds((st - 1) * (TILES * P), TILES * P)
                sp.wait_ge(y_ready, st)
                sp.dma_start(x_tile[:], x[rows, :].rearrange("(t p) d -> p t d", p=P)).then_inc(x_tile_loaded, 16)

            sp.dma_start(wp_sb[:], w_proj).then_inc(w_proj_loaded, 16)
            load_x(0)
            for k in range(1, CHUNKS):
                load_x(k)
                load_unit(0, 0, SQUARE_ORDER[0][k - 1], first=True)
            load_unit(0, 0, SQUARE_ORDER[0][TILES - 1], first=True)
            for gc in range(1, CHUNKS):
                for t in range(TILES):
                    load_unit(0, gc, t, first=gc < 2)
            with sp.Fori(1, SUPERS) as st:
                for gc in range(CHUNKS):
                    for t in range(TILES):
                        load_unit(st, gc, t, first=False)
                    if gc == 1:
                        load_x_tile(st)
            load_x_tile(SUPERS)

            sp.wait_ge(over_ready, 1)
            general = sp.value_load(over[0:1, 0:1], min_val=0, max_val=1)
            with sp.If(general > 0):
                sp.wait_ge(stored, (SUPERS + 1) * 16)
                with sp.Fori(0, ALL_TILES) as tile:
                    sp.wait_ge(gen_stored, tile * 16 + 16)
                    sp.dma_start(gen_sq, adj[bass.ds(tile * P, P), :]).then_inc(gen_loaded, 16)
                    sp.dma_start(x_tile[:, 0, :], x[bass.ds(tile * P, P), :]).then_inc(gen_loaded, 16)
                    sp.wait_ge(gen_normed, tile + 1)
                    sp.dma_start(out[bass.ds(tile * P, P), :], out_tile[:, 0, :]).then_inc(gen_stored, 16)
                sp.wait_ge(gen_stored, (ALL_TILES + 1) * 16)

        @block.gpsimd
        def _(pool):
            pool.memset(ident[:], 0.0).then_inc(ident_zero, 1)
            pool.memset(minus_half[:], -0.5).then_inc(half_const, 1)
            pool.memset(minus_one[:], -1.0).then_inc(half_const, 1)
            pool.memset(eps_tile[:], EPS).then_inc(half_const, 1)
            pool.wait_ge(ident_zero, 1)
            pool.affine_select(out=ident[:], in_=ident[:], compare_op=ALU.not_equal, fill=1.0, base=0,
                               pattern=[[-1, P]], channel_multiplier=1).then_inc(ident_ready, 1)
            pool.wait_ge(half_const, 3)
            pool.sem_inc(y_ready, 1)
            pool.sem_inc(feat_turned, 1)
            pool.sem_inc(stored, 16)
            pool.sem_inc(feat_ready, 1)
            pool.sem_inc(gen_copied, 1)
            pool.sem_inc(gen_stored, 16)

            def finish_rows(st):
                pool.wait_ge(feat_ready, st + 2)
                pool.wait_ge(x_tile_loaded, st * 16 + 16)
                pool.wait_ge(stored, st * 16 + 16)
                pool.tensor_tensor(y_tile[:].rearrange("p t d -> p (t d)"), feat[:],
                                   x_tile[:].rearrange("p t d -> p (t d)"), ALU.add).then_inc(y_ready, 1)
                pool.wait_ge(mean_ready, st * TILES + TILES)
                pool.tensor_tensor(var_eps[:], mean_var[:, :, 1], eps_tile[:], ALU.add).then_inc(eps_added, 1)
                pool.wait_ge(eps_added, st + 1)
                pool.tensor_tensor(rstd[:], var_eps[:], minus_half[:], ALU.pow).then_inc(rstd_ready, 1)
                pool.tensor_tensor(minus_mean[:], mean_var[:, :, 0], minus_one[:], ALU.mult
                                   ).then_inc(minus_mean_ready, 1)
                pool.wait_ge(rstd_ready, st + 1)
                pool.wait_ge(minus_mean_ready, st + 1)
                pool.tensor_tensor(shift[:], minus_mean[:], rstd[:], ALU.mult).then_inc(shift_ready, 1)

            with pool.Fori(0, SUPERS) as st:
                finish_rows(st)
            pool.wait_ge(max_ready, 1)
            pool.partition_all_reduce(count_top[:], count_max[:], P, bass.bass_isa.ReduceOp.max).then_inc(top_ready, 1)

            pool.wait_ge(over_ready, 1)
            general = pool.value_load(over[0:1, 0:1], min_val=0, max_val=1)
            with pool.If(general > 0):
                with pool.Fori(0, ALL_TILES) as tile:
                    pool.wait_ge(gen_mean, tile + 1)
                    pool.tensor_tensor(var_eps[:, 0:1], mean_var[:, 0, 1:2], eps_tile[:, 0:1], ALU.add
                                       ).then_inc(gen_eps, 1)
                    pool.wait_ge(gen_eps, tile + 1)
                    pool.tensor_tensor(rstd[:, 0:1], var_eps[:, 0:1], minus_half[:, 0:1], ALU.pow
                                       ).then_inc(gen_rstd, 1)

        @block.scalar
        def _(act):
            act.dma_start(bp_sb[:], b_proj.rearrange("(p o) -> p o", o=1)).then_inc(biases_loaded, 16)
            act.dma_start(wg_sb[:], w_gcn).then_inc(w_gcn_loaded, 16)
            act.dma_start(bg_sb[:], b_gcn.rearrange("(p o) -> p o", o=1)).then_inc(biases_loaded, 16)
            act.wait_ge(biases_loaded, 32)

            def tanh_h(n):
                act.wait_ge(proj_done, n + 1)
                if n >= 2:
                    act.wait_ge(gcn_done, n - 1)
                act.activation(h2T[:, n % 2, :], (ps_acc, ps_proj)[n % 2][:], ACT.Tanh, bias=bp_sb[:, 0:1]
                               ).then_inc(h2T_ready, 1)

            def keep_g(n):
                act.wait_ge(gcn_done, n + 1)
                lo = 1024 + (n % 2) * 512
                act.activation(g_sb[:, n // 4, 4 * (n % 4):4 * (n % 4) + 4, :],
                               ps_turn[:, lo:lo + 512].rearrange("p (c d) -> p c d", d=D), ACT.Copy
                               ).then_inc(g_ready, 1)

            def tanh_unit(st, gc, t):
                if t in VEC[gc]:
                    n = VEC[gc].index(t)
                    act.wait_ge(vec_turned, vec_unit(st, gc, n) + 1)
                    src = sqT[:, vec_unit(0, gc, n) % SQ_BUFS, :].rearrange("p (r c a) -> p c r a", r=Q, c=BLOCKS)
                    act.activation(adjT[:, gc % 2, :, t, :].rearrange("p c (r a) -> p c r a", r=Q), src,
                                   ACT.Tanh).then_inc(tanh_of_vec, 1)
                else:
                    n = PET[gc].index(t)
                    act.wait_ge(pe_turned, pe_unit(st, gc, n) + 1)
                    act.activation(adjT[:, gc % 2, :, t, :], ps_turn[:].rearrange("p (c i) -> p c i", c=BLOCKS),
                                   ACT.Tanh).then_inc(tanh_of_pe, 1)

            for n in range(PIECES + 2):
                if n < PIECES:
                    tanh_h(n)
                if 1 <= n <= PIECES:
                    keep_g(n - 1)
                if n in TANH_EARLY:
                    tanh_unit(0, 0, VEC[0][TANH_EARLY.index(n)])

            def tanh_group(st, gc, no_user):
                if not no_user:
                    act.wait_ge(group_used, group(st, gc) - 1)
                if no_user and gc == 1:
                    act.wait_ge(x_turned, PIECES)
                order = [VEC[gc][0]] + [t for pair in zip(PET[gc], VEC[gc][1:]) for t in pair]
                order += [t for t in range(TILES) if t not in order]
                if no_user and gc == 0:
                    order = [t for t in order if t not in VEC[0][:len(TANH_EARLY)]]
                for t in order:
                    tanh_unit(st, gc, t)

            def count_group(st, gc):
                for h in range(2):
                    lo = ((gc % 2) * TILES + 2 * h) * CHUNK
                    pair = slots[:, lo:lo + 2 * CHUNK]
                    act.activation(pair, pair, ACT.Sign,
                                   accum_out=counts[:, bass.ds(group(st, gc) * 2 + h, 1)]).then_inc(counted, 1)

            def read_products(st):
                act.wait_ge(group_used, st * CHUNKS)
                act.wait_ge(feat_turned, st)
                act.activation(featT[:], ps_acc[:], ACT.Identity, bias=bg_sb[:, 0:1]).then_inc(acc_read, 1)

            def relu_feat(st):
                act.wait_ge(feat_turned, st + 1)
                act.wait_ge(y_ready, st)
                act.activation(feat[:], ps_epi[:], ACT.Relu).then_inc(feat_ready, 1)

            def norm_and_store(st):
                act.wait_ge(shift_ready, st)
                act.wait_ge(stored, st * 16)
                for t in range(TILES):
                    ins = act.activation(out_tile[:, t, :], y_tile[:, t, :], ACT.Identity, bias=shift[:, t:t + 1],
                                         scale=rstd[:, t:t + 1])
                ins.then_inc(normed, 1)
                act.wait_ge(normed, st)
                rows = bass.ds((st - 1) * (TILES * P), TILES * P)
                act.dma_start(out[rows, :].rearrange("(t p) d -> p t d", p=P), out_tile[:]).then_inc(stored, 16)

            def super_tile(st, first):
                for gc in range(CHUNKS):
                    if gc == 1 and not first:
                        read_products(st)
                    if gc == 2 and not first:
                        relu_feat(st)
                    tanh_group(st, gc, no_user=first and gc < 2)
                    count_group(st, gc)
                if not first:
                    norm_and_store(st)

            super_tile(0, True)
            with act.Fori(1, SUPERS) as st:
                super_tile(st, False)
            read_products(SUPERS)
            relu_feat(SUPERS)
            norm_and_store(SUPERS)
            act.wait_ge(stored, (SUPERS + 1) * 16)

            act.wait_ge(over_ready, 1)
            general = act.value_load(over[0:1, 0:1], min_val=0, max_val=1)
            with act.If(general > 0):
                with act.Fori(0, ALL_TILES) as tile:
                    act.wait_ge(gen_squared, tile + 1)
                    act.activation(gen_filt, gen_sq, ACT.Tanh).then_inc(gen_tanh, 1)
                    act.activation(gen_rest[:, DUMMIES:], gen_sq, ACT.Tanh).then_inc(gen_tanh, 1)
                    for k in range(CHUNKS):
                        act.wait_ge(gen_turned, tile * CHUNKS + k + 1)
                        act.activation(gen_adjT[:, k * CHUNK:(k + 1) * CHUNK], ps_turn[:], ACT.Copy
                                       ).then_inc(gen_copied, 1)

        @block.tensor
        def _(pe):
            def turn_x(n):
                k, c0 = n // 4, 4 * (n % 4)
                pe.wait_ge(x_in_loaded[k], 16)
                if n >= 2:
                    pe.wait_ge(xT_ready, n - 1)
                for c in range(4):
                    mm = pe.transpose(ps_turn[:, (n % 2) * 512 + c * P:(n % 2) * 512 + (c + 1) * P],
                                      x_in[:, k * BLOCKS + c0 + c, :], ident[:])
                mm.then_inc(x_turned, 1)

            def project(n):
                pe.wait_ge(xT_ready, n + 1)
                if n == 0:
                    pe.wait_ge(w_proj_loaded, 16)
                if n >= 2:
                    pe.wait_ge(h2T_ready, n - 1)
                pe.matmul((ps_acc, ps_proj)[n % 2][:], wp_sb[:], xT[:, n % 2, :], start=True, stop=True
                          ).then_inc(proj_done, 1)

            def gcn(n):
                pe.wait_ge(h2T_ready, n + 1)
                if n == 0:
                    pe.wait_ge(w_gcn_loaded, 16)
                if n >= 2:
                    pe.wait_ge(g_ready, n - 1)
                for c in range(4):
                    lo = 1024 + (n % 2) * 512 + c * P
                    mm = pe.matmul(ps_turn[:, lo:lo + P], h2T[:, n % 2, c * P:(c + 1) * P], wg_sb[:],
                                   start=True, stop=True)
                mm.then_inc(gcn_done, 1)

            pe.wait_ge(ident_ready, 1)
            for n in range(PIECES + 2):
                if n < PIECES:
                    turn_x(n)
                if 1 <= n <= PIECES:
                    project(n - 1)
                if n >= 2:
                    gcn(n - 2)

            def turn_unit(st, gc, n, first):
                t = PET[gc][n]
                pe.wait_ge(squared, group(st, gc) * TILES + SQUARE_ORDER[gc].index(t) + 1)
                if not (first and n == 0):
                    pe.wait_ge(tanh_of_pe, pe_unit(st, gc, n))
                cols = slot_of(gc, t).rearrange("p (j c) -> p c j", c=BLOCKS)
                for c in range(BLOCKS):
                    mm = pe.transpose(ps_turn[:, c * P:(c + 1) * P], cols[:, c, :], ident[:])
                mm.then_inc(pe_turned, 1)

            def begin_products(st, gc):
                k = (gc - 1) % CHUNKS
                pe.wait_ge(tanh_of_pe, pe_unit(st, gc, 0))
                pe.wait_ge(tanh_of_vec, vec_unit(st, gc, 0))
                if k == 0 and not isinstance(st, int):
                    pe.wait_ge(acc_read, st)

            def multiply(gc, c):
                k = (gc - 1) % CHUNKS
                mm = pe.matmul(ps_acc[:], g_sb[:, k, c, :],
                               adjT[:, (gc - 1) % 2, c].rearrange("p t i -> p (t i)"),
                               start=(k == 0 and c == 0), stop=(k == CHUNKS - 1 and c == BLOCKS - 1))
                if c == BLOCKS - 1:
                    mm.then_inc(group_used, 1)

            def turn_feat(st):
                pe.wait_ge(acc_read, st)
                pe.wait_ge(feat_ready, st)
                for t in range(TILES):
                    mm = pe.transpose(ps_epi[:, t * P:(t + 1) * P], featT[:, t * P:(t + 1) * P], ident[:])
                mm.then_inc(feat_turned, 1)

            def super_tile(st, first):
                for gc in range(CHUNKS):
                    for c in range(BLOCKS):
                        if gc == 1 and c == BLOCKS // 2 and not first:
                            turn_feat(st)
                        if c in TURN_AT and TURN_AT.index(c) < len(PET[gc]):
                            turn_unit(st, gc, TURN_AT.index(c), first=first and gc == 0)
                        if not (first and gc == 0):
                            if c == 0:
                                begin_products(st, gc)
                            multiply(gc, c)

            pe.wait_ge(g_ready, PIECES)
            super_tile(0, True)
            with pe.Fori(1, SUPERS) as st:
                super_tile(st, False)
            begin_products(SUPERS, 0)
            for c in range(BLOCKS):
                multiply(0, c)
            turn_feat(SUPERS)

            pe.wait_ge(over_ready, 1)
            general = pe.value_load(over[0:1, 0:1], min_val=0, max_val=1)
            with pe.If(general > 0):
                with pe.Fori(0, ALL_TILES) as tile:
                    pe.wait_ge(gen_kept, tile + 1)
                    for k in range(CHUNKS):
                        pe.wait_ge(gen_copied, tile * CHUNKS + k + 1)
                        cols = gen_filt[:, k * CHUNK:(k + 1) * CHUNK].rearrange("p (j c) -> p c j", c=BLOCKS)
                        for c in range(BLOCKS):
                            mm = pe.transpose(ps_turn[:, c * P:(c + 1) * P], cols[:, c, :], ident[:])
                        mm.then_inc(gen_turned, 1)
                    pe.wait_ge(gen_copied, tile * CHUNKS + CHUNKS + 1)
                    for k in range(CHUNKS):
                        for c in range(BLOCKS):
                            lo = (k * BLOCKS + c) * P
                            mm = pe.matmul(ps_acc[:, 0:P], g_sb[:, k, c, :], gen_adjT[:, lo:lo + P],
                                           start=(k == 0 and c == 0),
                                           stop=(k == CHUNKS - 1 and c == BLOCKS - 1))
                    mm.then_inc(gen_products, 1)
                    pe.wait_ge(gen_feat, tile + 1)
                    pe.transpose(ps_epi[:, 0:P], featT[:, 0:P], ident[:]).then_inc(gen_feat_turned, 1)

        @block.vector
        def _(dve):
            def square(st, gc, t):
                s = (gc % 2) * TILES + t
                loads = [16 * (Q if t in VEC[k] else 1) for k in range(gc % 2, CHUNKS, 2)]
                dve.wait_ge(unit_loaded[s], st * sum(loads) + sum(loads[:gc // 2 + 1]))
                dve.scalar_tensor_tensor(out=slot_of(gc, t), in0=slot_of(gc, t), scalar=0.0, in1=slot_of(gc, t),
                                         op0=ALU.max, op1=ALU.mult).then_inc(squared, 1)

            def turn(st, gc, t):
                k = vec_unit(0, gc, VEC[gc].index(t))
                dve.wait_ge(squared, group(st, gc) * TILES + SQUARE_ORDER[gc].index(t) + 1)
                last = k - SQ_BUFS
                if last < 0 and not isinstance(st, int):
                    last = max(j for j in range(NV) if j % SQ_BUFS == k % SQ_BUFS) - NV
                if isinstance(st, int) and k == SQ_BUFS - 1:
                    dve.wait_ge(gcn_done, PIECES)
                elif last >= 0 or not isinstance(st, int):
                    dve.wait_ge(tanh_of_vec, st * NV + last + 1)
                dve.transpose(sqT[:, k % SQ_BUFS, :].rearrange("p (r c a) -> p r c a", r=Q, c=BLOCKS),
                              slot_of(gc, t).rearrange("p (r b c) -> p r c b", r=Q, c=BLOCKS)
                              ).then_inc(vec_turned, 1)

            def row_stats(st):
                dve.wait_ge(y_ready, st + 1)
                for t in range(TILES):
                    dve.bn_stats(stats[:, t, :], y_tile[:, t, :]).then_inc(stats_ready, 1)
                dve.wait_ge(stats_ready, st * TILES)
                dve.memset(wait_pad[:], 0.0)
                for t in range(TILES):
                    dve.bn_aggr(mean_var[:, t, :], stats[:, t, :]).then_inc(mean_ready, 1)

            def copy_xT(n):
                dve.wait_ge(x_turned, n + 1)
                if n >= 2:
                    dve.wait_ge(proj_done, n - 1)
                dve.tensor_copy(xT[:, n % 2, :], ps_turn[:, (n % 2) * 512:(n % 2) * 512 + 512]
                                ).then_inc(xT_ready, 1)

            def steps_of(gc):
                steps, late = [], None
                for t in SQUARE_ORDER[gc]:
                    steps.append((square, t))
                    if late is not None:
                        steps.append((turn, late))
                    late = t if t in VEC[gc] else None
                return steps + [(turn, late)]

            early = steps_of(0)
            for n in range(PIECES):
                copy_xT(n)
                if n in VEC_EARLY:
                    step, t = early.pop(0)
                    step(0, 0, t)
            for step, t in early:
                step(0, 0, t)

            def super_tile(st, first):
                for gc in range(1 if first else 0, CHUNKS):
                    for step, t in steps_of(gc):
                        step(st, gc, t)
                    if gc == 3 and not first:
                        row_stats(st)

            super_tile(0, True)
            with dve.Fori(1, SUPERS) as st:
                super_tile(st, False)
            row_stats(SUPERS)
            dve.wait_ge(counted, GROUPS * 2)
            dve.tensor_reduce(count_sums[:], counts[:].rearrange("p (s k t) -> p s t k", k=CHUNKS, t=2),
                              AX.X, ALU.add).then_inc(sums_ready, 1)
            dve.wait_ge(sums_ready, 1)
            dve.tensor_reduce(count_max[:], count_sums[:].rearrange("p s t -> p (s t)"), AX.X, ALU.max
                              ).then_inc(max_ready, 1)
            dve.wait_ge(top_ready, 1)
            dve.tensor_scalar(over[:], count_top[:], SURE + 0.5, None, ALU.is_gt).then_inc(over_ready, 1)

            dve.wait_ge(over_ready, 1)
            dve.wait_ge(stored, (SUPERS + 1) * 16)
            general = dve.value_load(over[0:1, 0:1], min_val=0, max_val=1)
            with dve.If(general > 0):
                with dve.Fori(0, ALL_TILES) as tile:
                    dve.wait_ge(gen_loaded, tile * 32 + 32)
                    if DUMMIES:
                        dve.memset(gen_rest[:, 0:DUMMIES], 2.0)
                    dve.scalar_tensor_tensor(out=gen_sq, in0=gen_sq, scalar=0.0, in1=gen_sq,
                                             op0=ALU.max, op1=ALU.mult).then_inc(gen_squared, 1)
                    dve.wait_ge(gen_tanh, tile * 2 + 2)
                    dve.memset(wait_pad[:], 0.0)
                    with dve.Fori(0, ROUNDS) as rnd:
                        dve.max(top8[:], gen_rest).then_inc(gen_top8, 1)
                        dve.wait_ge(gen_top8, tile * ROUNDS + rnd + 1)
                        dve.memset(wait_pad[:], 0.0)
                        dve.match_replace(gen_rest, top8[:], gen_rest, 0.0).then_inc(gen_taken, 1)
                        dve.wait_ge(gen_taken, tile * ROUNDS + rnd + 1)
                        dve.memset(wait_pad[:], 0.0)
                    dve.tensor_tensor(gen_filt, gen_filt, gen_rest[:, DUMMIES:], ALU.subtract
                                      ).then_inc(gen_kept, 1)
                    dve.wait_ge(gen_products, tile + 1)
                    dve.tensor_scalar(featT[:, 0:P], ps_acc[:, 0:P], bg_sb[:, 0:1], None, ALU.add
                                      ).then_inc(gen_feat, 1)
                    dve.wait_ge(gen_feat_turned, tile + 1)
                    dve.scalar_tensor_tensor(out=y_tile[:, 0, :], in0=ps_epi[:, 0:P], scalar=0.0,
                                             in1=x_tile[:, 0, :], op0=ALU.max, op1=ALU.add).then_inc(gen_y, 1)
                    dve.wait_ge(gen_y, tile + 1)
                    dve.bn_stats(stats[:, 0, :], y_tile[:, 0, :]).then_inc(gen_stats, 1)
                    dve.wait_ge(gen_stats, tile + 1)
                    dve.memset(wait_pad[:], 0.0)
                    dve.bn_aggr(mean_var[:, 0, :], stats[:, 0, :]).then_inc(gen_mean, 1)
                    dve.wait_ge(gen_rstd, tile + 1)
                    dve.wait_ge(gen_mean, tile + 1)
                    dve.tensor_scalar(out_tile[:, 0, :], y_tile[:, 0, :], mean_var[:, 0, 0:1], rstd[:, 0:1],
                                      ALU.subtract, ALU.mult).then_inc(gen_normed, 1)


_INS = ['x', 'adj', 'L0_gnn_W_proj', 'L0_gnn_b_proj', 'L0_gnn_W_gcn', 'L0_gnn_b_gcn']
_OUTS = [((8192, 128), 'float32')]


def kernel(**inputs):
    import numpy as _np
    import concourse.bacc as _bacc
    from concourse import mybir as _mybir
    from concourse.bass_utils import run_bass_kernel_spmd as _run

    nc = _bacc.Bacc("TRN2", target_bir_lowering=False, num_devices=1)
    arrays, args = {}, []
    for name in _INS:
        a = _np.ascontiguousarray(inputs[name])
        arrays[f"in_{name}_dram"] = a
        args.append(nc.dram_tensor(f"in_{name}_dram", a.shape, _mybir.dt.from_np(a.dtype), kind="ExternalInput").ap())
    for i, (shape, dtype) in enumerate(_OUTS):
        dt = _mybir.dt.from_np(_np.dtype(dtype))
        args.append(nc.dram_tensor(f"out_{i}_dram", shape, dt, kind="ExternalOutput").ap())
    graph_layer_kernel(nc, *args)
    r = _run(nc, [arrays], core_ids=[0])
    got = tuple(r.results[0][f"out_{i}_dram"] for i in range(len(_OUTS)))
    return got[0]
```
